# Optimizing a Trainium2 kernel written in Bass

```python
import numpy as np
import jax
import jax.numpy as jnp

def _softmax(x, axis=-1):
    return jax.nn.softmax(x, axis=axis)
def _gelu(x):
    return jax.nn.gelu(x, approximate=True)
def _silu(x):
    return jax.nn.silu(x)
def _sigmoid(x):
    return jax.nn.sigmoid(x)
def _layernorm(x, axis=-1, eps=1e-5):
    m = jnp.mean(x, axis=axis, keepdims=True)
    v = jnp.var(x, axis=axis, keepdims=True)
    return (x - m) / jnp.sqrt(v + eps)
def _scatter_add(tgt, idx, src, axis=0):
    return tgt.at[idx].add(src)
def _segment_sum(src, seg, n):
    return jax.ops.segment_sum(src, seg, n)

kernel_name = 'mk_conv_seq_d1_conv_nchw512_be1c3b'

def setup_inputs(seed: int = 0):
    np.random.seed(seed)
    _w = jnp.asarray
    def _rec_inputs():
        import jax
        import jax.numpy as jnp
        _gk = jax.random.key(seed)
        x = 7.22e-05 + 1 * jax.random.normal(jax.random.fold_in(_gk, 1), (16, 512, 32, 32), jnp.float32)
        return x
    x = _rec_inputs()
    def _L0_conv_setup():
        import jax, jax.numpy as jnp
        import numpy as np
        EPS_W = 0.0001
        EPS_PIX = 1e-08
        B_CONTRIB = 0.3

        def normalize_weight(w, eps=EPS_W):
            O = w.shape[0]
            fan_in = w.size // O
            wf = w.reshape(O, fan_in)
            n = jnp.linalg.norm(wf, axis=1, keepdims=True)
            alpha = np.float32(np.sqrt(1.0 / fan_in, dtype=np.float32))
            return (wf / (eps + alpha * n)).reshape(w.shape)

        def pixnorm(x, eps=EPS_PIX):
            return x / jnp.sqrt(jnp.mean(x * x, axis=-1, keepdims=True) + eps)
        key = jax.random.key(seed)
        k1, k2, k3 = jax.random.split(key, 3)
        B, C, H, W = (16, 512, 32, 32)
        x = jax.random.normal(k1, (B, C, H, W), dtype=jnp.float32)
        w_proj = jax.random.normal(k2, (3 * C, C, 1, 1), dtype=jnp.float32)
        w_out = jax.random.normal(k3, (C, C, 1, 1), dtype=jnp.float32)
        return {'x': x, 'w_proj': w_proj, 'w_out': w_out}
    _L0_conv_all = _L0_conv_setup()
    _L0_conv_in = {k: v for k, v in _L0_conv_all.items() if k in ('w_proj', 'w_out', )}
    del _L0_conv_all

    return {
        "x": x,
        "L0_conv_w_proj": _L0_conv_in["w_proj"],
        "L0_conv_w_out": _L0_conv_in["w_out"],
    }

def reference(x, L0_conv_w_proj, L0_conv_w_out):
    import jax
    import jax.numpy as jnp
    def _L0_conv_ref(x, w_proj, w_out):
        import jax, jax.numpy as jnp
        import numpy as np
        EPS_W = 0.0001
        EPS_PIX = 1e-08
        B_CONTRIB = 0.3

        def normalize_weight(w, eps=EPS_W):
            O = w.shape[0]
            fan_in = w.size // O
            wf = w.reshape(O, fan_in)
            n = jnp.linalg.norm(wf, axis=1, keepdims=True)
            alpha = np.float32(np.sqrt(1.0 / fan_in, dtype=np.float32))
            return (wf / (eps + alpha * n)).reshape(w.shape)

        def pixnorm(x, eps=EPS_PIX):
            return x / jnp.sqrt(jnp.mean(x * x, axis=-1, keepdims=True) + eps)
        B, C, H, W = x.shape
        N = H * W
        d_k = 64
        n_heads = C // d_k
        scale = np.float32(1.0 / np.sqrt(np.sqrt(d_k)))
        fan_in = np.float32(np.sqrt(C, dtype=np.float32))
        wp = normalize_weight(w_proj)[:, :, 0, 0] / fan_in
        wo = normalize_weight(w_out)[:, :, 0, 0] / fan_in
        xf = x.reshape(B, C, N)
        h = jnp.einsum('oc,bcn->bno', wp, xf)
        qkv = h.reshape(B, N, n_heads, 3 * d_k)
        q, k, v = jnp.split(qkv, 3, axis=-1)
        q = pixnorm(q) * scale
        k = pixnorm(k) * scale
        v = pixnorm(v)
        attn = jnp.einsum('bihd,bjhd->bijh', q, k)
        attn = jax.nn.softmax(attn, axis=2)
        res = jnp.einsum('bijh,bjhd->bihd', attn, v)
        res = res.reshape(B, N, C)
        res = jnp.einsum('oc,bnc->bon', wo, res).reshape(B, C, H, W)
        a_c = np.float32(1.0 - B_CONTRIB)
        b_c = np.float32(B_CONTRIB)
        div = np.float32(np.sqrt(a_c * a_c + b_c * b_c, dtype=np.float32))
        return (a_c * x + b_c * res) / div

    def _gn(v, G=32, eps=1e-5):
        B_, C_, H_, W_ = v.shape
        g = v.reshape(B_, G, C_ // G, H_, W_)
        m = jnp.mean(g, axis=(2, 3, 4), keepdims=True)
        s = jnp.var(g, axis=(2, 3, 4), keepdims=True)
        return ((g - m) / jnp.sqrt(s + eps)).reshape(v.shape)

    def _ln_c(v, eps=1e-6):
        m = jnp.mean(v, axis=1, keepdims=True)
        s = jnp.var(v, axis=1, keepdims=True)
        return (v - m) / jnp.sqrt(s + eps)

    def _ln_t(v, eps=1e-5):
        m = jnp.mean(v, axis=-1, keepdims=True)
        s = jnp.var(v, axis=-1, keepdims=True)
        return (v - m) / jnp.sqrt(s + eps)

    def _to_tokens(v):
        B_, C_, H_, W_ = v.shape
        return v.reshape(B_, C_, H_ * W_).transpose(0, 2, 1)
    def _from_tokens(t, like):
        B_, C_, H_, W_ = like.shape
        return t.transpose(0, 2, 1).reshape(B_, C_, H_, W_)

    x = _L0_conv_ref(x, L0_conv_w_proj, L0_conv_w_out)
    return x


_drawn_inputs = setup_inputs


def setup_inputs(seed=0):
    import zlib

    import numpy as np

    out = dict(_drawn_inputs(seed))
    spreads = {}
    factors = {}
    for name, (base, spread) in spreads.items():
        noise = np.random.default_rng([zlib.crc32(name.encode()), seed]).standard_normal(out[name].shape)
        drawn = base * np.exp(spread * noise) if base else spread * noise
        out[name] = jnp.asarray(drawn.astype(out[name].dtype))
    for name, factor in factors.items():
        out[name] = (out[name] * factor).astype(out[name].dtype)
    return out
```

```python
from contextlib import ExitStack
from math import sqrt

import numpy as np

import concourse.bass as bass
from concourse import mybir

F32 = mybir.dt.float32
F32R = mybir.dt.float32r
F16 = mybir.dt.float16
I32 = mybir.dt.int32
ACT = mybir.ActivationFunctionType
ALU = mybir.AluOpType
AX = mybir.AxisListType

P = 128
B, C, H, W = 16, 512, 32, 32
N = H * W
D = 64
HEADS = C // D
PAIRS = HEADS // 2
O3 = 3 * C
CT = C // P
NT = N // P
NH = 512
PAIR_O = 6 * D

EPS_W = 1e-4
EPS_PIX = 1e-8
B_CONTRIB = 0.3
A_C, B_C = np.float32(1.0 - B_CONTRIB), np.float32(B_CONTRIB)
DIV = float(np.sqrt(A_C * A_C + B_C * B_C, dtype=np.float32))
FAN_IN = float(np.sqrt(C, dtype=np.float32))
ALPHA = float(np.sqrt(1.0 / C, dtype=np.float32))
QK_SCALE = 1.0 / sqrt(sqrt(D))

QK_UP = 2.0 ** 10
V_UP = 2.0 ** 12
WO_UP = 2.0 ** 14
PROB_SHIFT = 3.0
RSQRT_SEED = 1597463007.0

SLOTS = 64
UNIT_SLOTS = 4
HEAD_SLOTS = 8
PAIR_SLOTS = 16

PROJ_AT = [PAIR_SLOTS * p - 24 + o for p in range(PAIRS) for o in (0, 1, 3, 4, 6, 7, 9, 10)]
NORM_AT = [PAIR_SLOTS * p - 13 for p in range(PAIRS)]
SCALE_AT = [PAIR_SLOTS * p - 12 + hh for p in range(PAIRS) for hh in range(2)]
HIGH_AT = [PAIR_SLOTS * p - 11 + hh for p in range(PAIRS) for hh in range(2)]
LOW_AT = [PAIR_SLOTS * p - 10 + hh for p in range(PAIRS) for hh in range(2)]
TURN_QK_AT = [PAIR_SLOTS * p + o for p in range(PAIRS) for o in (-7, -5, -3, 1, 3, 5)]
PV_LAG = 5
RES_AT = [UNIT_SLOTS * u + PV_LAG + 3 for u in range(2 * HEADS)]
TURN_RES_AT = [PAIR_SLOTS * p + 23 + o for p in range(PAIRS) for o in range(2)]
OUT_AT = [SLOTS + o for o in (10, 12, 14, 15, 16, 18, 20, 22)]
SPLIT_AT = [-29, -29, -28, -28, -27, -27, -26, -26]
FIRST_SLOT = -32
LAST_SLOT = SLOTS + 26


def prepare_and_attend(nc, x, w_proj, w_out, out):
    x_in = x.rearrange("b (t p) h w -> b t p (h w)", p=P)
    out_v = out.rearrange("b (t p) h w -> b t p (h w)", p=P)
    wp_in = w_proj.rearrange("(m p) c a b -> p m (c a b)", p=P)
    wo_in = w_out.rearrange("(m p) c a b -> p m (c a b)", p=P)
    WP_TILES, WO_TILES = O3 // P, C // P
    W_TILES = WP_TILES + WO_TILES
    W_GROUPS = W_TILES // 4

    with ExitStack() as ctx:
        def sb(name, shape, dt):
            return ctx.enter_context(nc.sbuf_tensor(name, shape, dt))

        def pb(name, shape, dt):
            return ctx.enter_context(nc.psum_tensor(name, shape, dt))

        def sem(name):
            return ctx.enter_context(nc.semaphore(name))

        wpT_hi = sb("wpT_hi", [P, CT, O3], F32R)
        wpT_lo = sb("wpT_lo", [P, CT, O3], F32R)
        woT_hi = sb("woT_hi", [P, CT, C], F16)
        woT_lo = sb("woT_lo", [P, CT, C], F16)
        ident32 = sb("ident32", [P, P], F32)
        ident16 = sb("ident16", [P, P], F16)
        x_raw = sb("x_raw", [P, 2, NH], F32)
        x_hi = sb("x_hi", [P, CT, N], F32R)
        x_lo = sb("x_lo", [P, CT, N], F32R)
        proj = sb("proj", [P, NT, PAIR_O], F32)
        squares = sb("squares", [P, 2, PAIR_O], F32)
        sumsq = sb("sumsq", [P, NT, 6], F32)
        rs = sb("rs", [P, NT, 6], F32)
        rs_t = sb("rs_t", [P, NT, 6], F32)
        rs_unit = sb("rs_unit", [P, NT, 6], F32)
        qk_pair = sb("qk_pair", [P, NT, 2, 5 * D], F16)
        qkT = sb("qkT", [P, 2, 3, N], F16)
        VCOLS = 2 * D + 1
        v_pair = sb("v_pair", [P, 4, NT, VCOLS + 1], F16)
        e_tile = sb("e_tile", [P, 2, 2, NH], F32)
        probs = sb("probs", [P, 2, 2, NT, NH], F16)
        pv_low = sb("pv_low", [P, 2, D], F32)
        pv_sum = sb("pv_sum", [P, 4, D], F32)
        inv_sum = sb("inv_sum", [P, 4], F32)
        res_pair = sb("res_pair", [P, 2, NT, 2 * D], F16)
        resT = sb("resT", [P, 2, CT, N], F16)
        x_res = sb("x_res", [P, 2, NH], F32)
        shift = sb("shift", [P, 1], F32)
        w_sumsq = sb("w_sumsq", [P, W_TILES], F32)
        w_rs = sb("w_rs", [P, W_TILES], F32)
        w_rs_t = sb("w_rs_t", [P, W_TILES], F32)
        w_raw = probs[:, :, :, :, :].rearrange("p a b j n -> p (a b j n)").bitcast(F32) \
            .rearrange("p (m c) -> p m c", c=C)
        w_scratch = e_tile[:, 0, 0, :]

        ps_score = pb("ps_score", [P, 2, 2, NH], F32)
        ps_pv = pb("ps_pv", [P, 2, NH], F32)
        ps_proj = pb("ps_proj", [P, NH], F32)
        ps_aux = pb("ps_aux", [P, NH], F32)
        ps_aux16 = ps_aux[:, :].bitcast(F16)

        w_loaded = [sem(f"w_loaded{g}") for g in range(W_GROUPS)]
        ident_made = sem("ident_made")
        consts_set = sem("consts_set")
        w_squared = sem("w_squared")
        w_step = sem("w_step")
        w_scaled = sem("w_scaled")
        w_turned = sem("w_turned")
        w_high = sem("w_high")
        w_low = sem("w_low")
        x_loaded = [sem(f"x_loaded{i}") for i in range(2)]
        x_high = sem("x_high")
        x_split = sem("x_split")
        proj_done = sem("proj_done")
        squared = sem("squared")
        proj_copied = sem("proj_copied")
        reduced = sem("reduced")
        norm_step = sem("norm_step")
        scaled = sem("scaled")
        qk_high = sem("qk_high")
        v_high = sem("v_high")
        qk_low = sem("qk_low")
        v_low = sem("v_low")
        qk_turned = sem("qk_turned")
        qkT_copied = sem("qkT_copied")
        scores_done = sem("scores_done")
        exp_done = sem("exp_done")
        probs_high = sem("probs_high")
        probs_low = sem("probs_low")
        pv_done = sem("pv_done")
        pv_low_copied = sem("pv_low_copied")
        pv_inverted = sem("pv_inverted")
        pv_added = sem("pv_added")
        res_scaled = sem("res_scaled")
        res_high = sem("res_high")
        res_low = sem("res_low")
        res_turned = sem("res_turned")
        resT_copied = sem("resT_copied")
        out_done = sem("out_done")
        x_res_loaded = [sem(f"x_res_loaded{i}") for i in range(2)]
        out_added = sem("out_added")
        out_scaled = sem("out_scaled")
        out_stored = [sem(f"out_stored{i}") for i in range(2)]

        def after(eng, semaphore, count):
            if isinstance(count, int) and count <= 0:
                return
            eng.wait_ge(semaphore, count)

        def timeline(eng, task):
            def body(b, prev=True, cur=True, nxt=True):
                for s in range(SLOTS):
                    if prev and s + SLOTS <= LAST_SLOT:
                        task(b - 1, s + SLOTS)
                    if cur:
                        task(b, s)
                    if nxt and s - SLOTS >= FIRST_SLOT:
                        task(b + 1, s - SLOTS)

            body(-1, prev=False, cur=False)
            body(0, prev=False)
            with eng.Fori(1, B - 1) as b:
                body(b)
            body(B - 1, nxt=False)
            body(B, cur=False, nxt=False)

        block = ctx.enter_context(nc.Block())

        @block.gpsimd
        def _(pool):
            pool.memset(ident32[:, :], 0.0).then_inc(ident_made, 1)
            pool.memset(ident16[:, :], 0.0).then_inc(ident_made, 1)
            pool.wait_ge(ident_made, 2)
            for t in (ident32, ident16):
                pool.affine_select(out=t[:, :], in_=t[:, :], compare_op=ALU.not_equal, fill=1.0, base=0,
                                   pattern=[[-1, P]], channel_multiplier=1).then_inc(ident_made, 1)

        @block.sync
        def _(sp):
            def load_x(b, piece):
                n = 8 * b + piece
                after(sp, x_split, n - 1)
                sp.dma_start(x_raw[:, piece % 2, :],
                             x_in[bass.ds(b, 1), piece // 2, :, (piece % 2) * NH:(piece % 2 + 1) * NH]
                             .rearrange("a p n -> p (a n)")).then_inc(x_loaded[piece % 2], 16)

            def load_residual(b, k):
                after(sp, out_stored[k % 2], 16 * (4 * b + k // 2))
                sp.dma_start(x_res[:, k % 2, :],
                             x_in[bass.ds(b, 1), k // 2, :, (k % 2) * NH:(k % 2 + 1) * NH]
                             .rearrange("a p n -> p (a n)")).then_inc(x_res_loaded[k % 2], 16)

            def store(b, k):
                sp.wait_ge(out_scaled, 8 * b + k + 1)
                sp.dma_start(out_v[bass.ds(b, 1), k // 2, :, (k % 2) * NH:(k % 2 + 1) * NH]
                             .rearrange("a p n -> p (a n)"),
                             x_res[:, k % 2, :]).then_inc(out_stored[k % 2], 16)

            def task(b, s):
                for piece, at in enumerate(SPLIT_AT):
                    if at - 2 == s:
                        load_x(b, piece)
                if s == OUT_AT[0] - 2:
                    load_residual(b, 0)
                    load_residual(b, 1)
                for k, at in enumerate(OUT_AT):
                    if at + 1 == s:
                        store(b, k)
                        if k + 2 < len(OUT_AT):
                            load_residual(b, k + 2)

            for g in range(W_GROUPS):
                src = wp_in[:, 4 * g:4 * g + 4, :] if 4 * g < WP_TILES else wo_in
                sp.dma_start(w_raw[:, 4 * g:4 * g + 4, :], src).then_inc(w_loaded[g], 16)
            timeline(sp, task)
            for i in range(2):
                sp.wait_ge(out_stored[i], 16 * 4 * B)

        @block.scalar
        def _(act):
            def square(b, n):
                act.wait_ge(proj_done, 32 * b + n + 1)
                after(act, reduced, 32 * b + n - 1)
                act.activation(squares[:, n % 2, :], ps_proj[:, 0:PAIR_O], ACT.Square).then_inc(squared, 1)

            def copy_proj(b, n):
                if n % NT == 0:
                    after(act, qk_low, 8 * b + 2 * (n // NT))
                    after(act, v_low, 8 * b + 2 * (n // NT))
                act.activation(proj[:, n % NT, :], ps_proj[:, 0:PAIR_O], ACT.Copy).then_inc(proj_copied, 1)

            def high(b, h):
                hh = h % 2
                act.wait_ge(scaled, 8 * b + h + 1)
                after(act, qk_turned, 3 * (8 * b + h - 1))
                src = proj[:, :, hh * 3 * D:(hh + 1) * 3 * D].rearrange("p n (g d) -> p n g d", d=D)
                act.activation(qk_pair[:, :, hh, 0:D], src[:, :, 0, :], ACT.Copy).then_inc(qk_high, 1)
                k_twice = qk_pair[:, :, hh, D:5 * D].rearrange("p n (e g d) -> p n e g d", g=2, d=D)
                act.activation(k_twice[:, :, :, 1, :], src[:, :, 1:2, :].broadcast_to([P, NT, 2, D]),
                               ACT.Copy).then_inc(qk_high, 1)
                after(act, pv_done, 8 * (8 * b + h - 3))
                act.activation(v_pair[:, h % 4, :, 0:D], src[:, :, 2, :], ACT.Copy).then_inc(v_high, 1)

            def copy_qkT(b, m):
                h, a = m // 3, m % 3
                act.wait_ge(qk_turned, 24 * b + m + 1)
                after(act, scores_done, 8 * (8 * b + h - 1))
                act.activation(qkT[:, h % 2, a, :], ps_aux16, ACT.Copy).then_inc(qkT_copied, 1)

            def exp(b, t):
                act.wait_ge(scores_done, SLOTS * b + t + 1)
                after(act, probs_low, SLOTS * b + t - 1)
                act.activation(e_tile[:, t % 2, :, :], ps_score[:, t % 2, :, :], ACT.Exp,
                               bias=shift[:, 0:1], scale=1.0 / (QK_UP * QK_UP)).then_inc(exp_done, 1)

            def copy_low(b, t):
                act.wait_ge(pv_done, SLOTS * b + t + 1)
                after(act, pv_added, SLOTS * b + t - 1)
                act.activation(pv_low[:, t % 2, :], ps_pv[:, t % 2, D + 1:VCOLS], ACT.Copy) \
                    .then_inc(pv_low_copied, 1)

            def finish(b, k):
                act.wait_ge(out_added, 8 * b + k + 1)
                act.activation(x_res[:, k % 2, :], x_res[:, k % 2, :], ACT.Copy,
                               scale=float(A_C) / DIV).then_inc(out_scaled, 1)

            def task(b, s):
                if 0 <= s - PV_LAG < SLOTS:
                    copy_low(b, s - PV_LAG)
                if 0 <= s < SLOTS:
                    exp(b, s)
                for n, at in enumerate(PROJ_AT):
                    if at == s:
                        square(b, n)
                        copy_proj(b, n)
                for h, at in enumerate(HIGH_AT):
                    if at == s:
                        high(b, h)
                for m, at in enumerate(TURN_QK_AT):
                    if at == s:
                        copy_qkT(b, m)
                for k, at in enumerate(OUT_AT):
                    if at + 1 == s:
                        finish(b, k)

            for m in range(W_TILES):
                act.wait_ge(w_loaded[m // 4], 16)
                if m:
                    act.wait_ge(w_squared, m)
                act.activation(w_scratch, w_raw[:, m, :], ACT.Square,
                               accum_out=w_sumsq[:, m:m + 1]).then_inc(w_squared, 1)
            for m in range(W_TILES):
                act.wait_ge(w_turned, m + 1)
                turned = ps_score[:, m % 2, 0, :].rearrange("p (t o) -> p t o", o=P)
                if m < WP_TILES:
                    act.activation(wpT_hi[:, :, m * P:(m + 1) * P], turned, ACT.Copy).then_inc(w_high, 1)
                else:
                    o = (m - WP_TILES) * P
                    act.activation(woT_hi[:, :, o:o + P], turned, ACT.Copy, scale=WO_UP).then_inc(w_high, 1)
            act.wait_ge(consts_set, 4)
            timeline(act, task)

        @block.vector
        def _(dve):
            def rsqrt(y, a, t, step, done):
                dve.tensor_scalar(y.bitcast(I32), a.bitcast(I32), -0.5, RSQRT_SEED, ALU.mult, ALU.add) \
                   .then_inc(step, 1)
                for i in range(4):
                    dve.wait_ge(step, done + 3 * i + 1)
                    dve.tensor_tensor(t, y, y, ALU.mult).then_inc(step, 1)
                    dve.wait_ge(step, done + 3 * i + 2)
                    dve.scalar_tensor_tensor(out=t, in0=t, scalar=-0.5, in1=a, op0=ALU.mult,
                                             op1=ALU.mult).then_inc(step, 1)
                    dve.wait_ge(step, done + 3 * i + 3)
                    dve.scalar_tensor_tensor(out=y, in0=t, scalar=1.5, in1=y, op0=ALU.add,
                                             op1=ALU.mult).then_inc(step, 1)
                dve.wait_ge(step, done + 13)
            RSQRT_STEPS = 13

            def split_x(b, piece):
                n = 8 * b + piece
                ct, half = piece // 2, slice((piece % 2) * NH, (piece % 2 + 1) * NH)
                dve.wait_ge(x_loaded[piece % 2], 16 * (4 * b + piece // 2 + 1))
                after(dve, proj_done, 32 * b)
                dve.tensor_copy(x_hi[:, ct, half], x_raw[:, piece % 2, :]).then_inc(x_high, 1)
                dve.wait_ge(x_high, n + 1)
                dve.tensor_tensor(x_lo[:, ct, half], x_raw[:, piece % 2, :],
                                  x_hi[:, ct, half].bitcast(F32), ALU.subtract).then_inc(x_split, 1)

            def reduce(b, n):
                dve.wait_ge(squared, 32 * b + n + 1)
                if n % NT == 0:
                    after(dve, norm_step, (RSQRT_STEPS + 2) * (4 * b + n // NT))
                dve.tensor_reduce(sumsq[:, n % NT, :],
                                  squares[:, n % 2, :].rearrange("p (g d) -> p g d", d=D), AX.X,
                                  ALU.add).then_inc(reduced, 1)

            def norms(b, p):
                dve.wait_ge(reduced, 32 * b + NT * (p + 1))
                after(dve, scaled, 8 * b + 2 * p)
                done = (RSQRT_STEPS + 2) * (4 * b + p)
                dve.tensor_scalar(sumsq[:, :, :], sumsq[:, :, :], D * EPS_PIX, None, ALU.add) \
                   .then_inc(norm_step, 1)
                dve.wait_ge(norm_step, done + 1)
                rsqrt(rs[:, :, :], sumsq[:, :, :], rs_t[:, :, :], norm_step, done + 1)
                dve.tensor_tensor(rs[:, :, :], rs[:, :, :], rs_unit[:, :, :], ALU.mult).then_inc(norm_step, 1)

            def scale(b, h):
                p, hh = h // 2, h % 2
                dve.wait_ge(proj_copied, 32 * b + NT * (p + 1))
                dve.wait_ge(norm_step, (RSQRT_STEPS + 2) * (4 * b + p + 1))
                v = proj[:, :, hh * 3 * D:(hh + 1) * 3 * D].rearrange("p n (g d) -> p n g d", d=D)
                r = rs[:, :, hh * 3:(hh + 1) * 3].unsqueeze(3).broadcast_to([P, NT, 3, D])
                dve.tensor_tensor(v, v, r, ALU.mult).then_inc(scaled, 1)

            def low(b, h):
                hh = h % 2
                src = proj[:, :, hh * 3 * D:(hh + 1) * 3 * D].rearrange("p n (g d) -> p n g d", d=D)
                dst = qk_pair[:, :, hh, 0:4 * D].rearrange("p n (g e d) -> p n g e d", e=2, d=D)
                dve.wait_ge(qk_high, 2 * (8 * b + h + 1))
                dve.tensor_tensor(dst[:, :, :, 1, :], src[:, :, 0:2, :], dst[:, :, :, 0, :],
                                  ALU.subtract).then_inc(qk_low, 1)
                dve.wait_ge(v_high, 8 * b + h + 1)
                dve.tensor_tensor(v_pair[:, h % 4, :, D + 1:VCOLS], src[:, :, 2, :],
                                  v_pair[:, h % 4, :, 0:D], ALU.subtract).then_inc(v_low, 1)

            def split_probs_high(b, t):
                u, k = t // UNIT_SLOTS, t % UNIT_SLOTS
                dve.wait_ge(exp_done, SLOTS * b + t + 1)
                if k == 0:
                    after(dve, pv_done, UNIT_SLOTS * (16 * b + u - 1))
                dve.tensor_copy(probs[:, u % 2, 0, 2 * k:2 * k + 2, :], e_tile[:, t % 2, :, :]) \
                   .then_inc(probs_high, 1)

            def split_probs_low(b, t):
                u, k = t // UNIT_SLOTS, t % UNIT_SLOTS
                dve.wait_ge(probs_high, SLOTS * b + t + 1)
                dve.tensor_tensor(probs[:, u % 2, 1, 2 * k:2 * k + 2, :], e_tile[:, t % 2, :, :],
                                  probs[:, u % 2, 0, 2 * k:2 * k + 2, :], ALU.subtract) \
                   .then_inc(probs_low, 1)

            def add_low(b, t):
                it = t % 4
                if it == 0:
                    after(dve, res_low, 16 * b + t // 4)
                dve.wait_ge(pv_low_copied, SLOTS * b + t + 1)
                dve.reciprocal(inv_sum[:, it:it + 1], ps_pv[:, t % 2, D:D + 1]).then_inc(pv_inverted, 1)
                dve.tensor_tensor(pv_sum[:, it, :], ps_pv[:, t % 2, 0:D], pv_low[:, t % 2, :],
                                  ALU.add).then_inc(pv_added, 1)

            def split_res(b, u):
                h, half = u // 2, u % 2
                cols = slice((h % 2) * D, (h % 2 + 1) * D)
                dve.wait_ge(pv_added, 4 * (16 * b + u + 1))
                dve.wait_ge(pv_inverted, 4 * (16 * b + u + 1))
                if u % 4 == 0:
                    after(dve, res_turned, 2 * (4 * b + u // 4))
                dve.tensor_tensor(pv_sum[:, :, :], pv_sum[:, :, :],
                                  inv_sum[:, :].unsqueeze(2).broadcast_to([P, 4, D]),
                                  ALU.mult).then_inc(res_scaled, 1)
                dve.wait_ge(res_scaled, 16 * b + u + 1)
                dve.tensor_copy(res_pair[:, 0, 4 * half:4 * half + 4, cols], pv_sum[:, :, :]) \
                   .then_inc(res_high, 1)
                dve.wait_ge(res_high, 16 * b + u + 1)
                dve.tensor_tensor(res_pair[:, 1, 4 * half:4 * half + 4, cols], pv_sum[:, :, :],
                                  res_pair[:, 0, 4 * half:4 * half + 4, cols],
                                  ALU.subtract).then_inc(res_low, 1)

            def copy_resT(b, m):
                dve.wait_ge(res_turned, 8 * b + m + 1)
                after(dve, out_done, 8 * b)
                dve.tensor_copy(resT[:, m % 2, m // 2, :], ps_aux16).then_inc(resT_copied, 1)

            def add_out(b, k):
                dve.wait_ge(out_done, 8 * b + k + 1)
                dve.wait_ge(x_res_loaded[k % 2], 16 * (4 * b + k // 2 + 1))
                dve.scalar_tensor_tensor(out=x_res[:, k % 2, :], in0=ps_aux[:, :],
                                         scalar=float(B_C) / float(A_C) / (V_UP * WO_UP),
                                         in1=x_res[:, k % 2, :], op0=ALU.mult,
                                         op1=ALU.add).then_inc(out_added, 1)

            def task(b, s):
                if 0 <= s - PV_LAG < SLOTS:
                    add_low(b, s - PV_LAG)
                if 0 <= s < SLOTS:
                    split_probs_high(b, s)
                    split_probs_low(b, s)
                for n, at in enumerate(PROJ_AT):
                    if at == s:
                        reduce(b, n)
                for p, at in enumerate(NORM_AT):
                    if at == s:
                        norms(b, p)
                for h, at in enumerate(SCALE_AT):
                    if at == s:
                        scale(b, h)
                for h, at in enumerate(LOW_AT):
                    if at == s:
                        low(b, h)
                for u, at in enumerate(RES_AT):
                    if at == s:
                        split_res(b, u)
                for m, at in enumerate(TURN_RES_AT):
                    if at == s:
                        copy_resT(b, m)
                for k, at in enumerate(OUT_AT):
                    if at == s:
                        add_out(b, k)
                for piece, at in enumerate(SPLIT_AT):
                    if at == s:
                        split_x(b, piece)

            dve.memset(v_pair[:, :, :, D:D + 1], 1.0).then_inc(consts_set, 1)
            dve.memset(shift[:, :], PROB_SHIFT).then_inc(consts_set, 1)
            unit = rs_unit[:, :, :].rearrange("p n (h g) -> p (n h) g", g=3)
            dve.memset(unit[:, :, 0:2], sqrt(D) * QK_SCALE * QK_UP).then_inc(consts_set, 1)
            dve.memset(unit[:, :, 2:3], sqrt(D) * V_UP).then_inc(consts_set, 1)
            dve.wait_ge(consts_set, 4)
            dve.wait_ge(w_squared, W_TILES)
            dve.tensor_scalar(w_sumsq[:, :], w_sumsq[:, :], 1e-30, None, ALU.max).then_inc(w_step, 1)
            dve.wait_ge(w_step, 1)
            rsqrt(w_rs[:, :], w_sumsq[:, :], w_rs_t[:, :], w_step, 1)
            n = 1 + RSQRT_STEPS
            dve.tensor_tensor(w_rs[:, :], w_rs[:, :], w_sumsq[:, :], ALU.mult).then_inc(w_step, 1)
            dve.wait_ge(w_step, n + 1)
            dve.tensor_scalar(w_rs[:, :], w_rs[:, :], ALPHA, EPS_W, ALU.mult, ALU.add).then_inc(w_step, 1)
            dve.wait_ge(w_step, n + 2)
            dve.tensor_scalar(w_rs[:, :], w_rs[:, :], FAN_IN, None, ALU.mult).then_inc(w_step, 1)
            dve.wait_ge(w_step, n + 3)
            dve.reciprocal(w_rs[:, :], w_rs[:, :]).then_inc(w_step, 1)
            dve.wait_ge(w_step, n + 4)
            for m in range(W_TILES):
                dve.tensor_scalar(w_raw[:, m, :], w_raw[:, m, :], w_rs[:, m:m + 1], None,
                                  ALU.mult).then_inc(w_scaled, 1)
            for m in range(W_TILES):
                dve.wait_ge(w_high, m + 1)
                turned = ps_score[:, m % 2, 0, :].rearrange("p (t o) -> p t o", o=P)
                if m < WP_TILES:
                    cols = slice(m * P, (m + 1) * P)
                    dve.tensor_tensor(wpT_lo[:, :, cols], turned, wpT_hi[:, :, cols].bitcast(F32),
                                      ALU.subtract).then_inc(w_low, 1)
                else:
                    cols = slice((m - WP_TILES) * P, (m - WP_TILES + 1) * P)
                    dve.scalar_tensor_tensor(out=woT_lo[:, :, cols], in0=turned, scalar=WO_UP,
                                             in1=woT_hi[:, :, cols], op0=ALU.mult,
                                             op1=ALU.subtract).then_inc(w_low, 1)
            dve.wait_ge(w_turned, W_TILES)
            timeline(dve, task)

        @block.tensor
        def _(pe):
            def project(b, n):
                p, nt = n // NT, n % NT
                if n == 0:
                    pe.wait_ge(x_split, 8 * (b + 1))
                after(pe, proj_copied, 32 * b + n)
                pix, cols = slice(nt * P, (nt + 1) * P), slice(p * PAIR_O, (p + 1) * PAIR_O)
                for ct in range(CT):
                    pe.matmul(ps_proj[:, 0:PAIR_O], x_hi[:, ct, pix], wpT_hi[:, ct, cols],
                              start=(ct == 0), stop=False)
                    pe.matmul(ps_proj[:, 0:PAIR_O], x_hi[:, ct, pix], wpT_lo[:, ct, cols],
                              start=False, stop=False)
                    mm = pe.matmul(ps_proj[:, 0:PAIR_O], x_lo[:, ct, pix], wpT_hi[:, ct, cols],
                                   start=False, stop=(ct == CT - 1))
                mm.then_inc(proj_done, 1)

            def aux_free(b, s):
                users = [(at, qkT_copied, 24, m + 1) for m, at in enumerate(TURN_QK_AT)]
                users += [(at, resT_copied, 8, m + 1) for m, at in enumerate(TURN_RES_AT)]
                users += [(at, out_added, 8, k + 1) for k, at in enumerate(OUT_AT)]
                past = [(at + SLOTS * e, copied, per, count, e) for at, copied, per, count in users
                        for e in (-1, 0, 1) if at + SLOTS * e < s
                        and not (isinstance(b, int) and not 0 <= b + e < B)]
                if past:
                    at, copied, per, count, e = max(past, key=lambda u: u[0])
                    pe.wait_ge(copied, per * (b + e) + count)

            def turn_qk(b, m, s):
                h, a = m // 3, m % 3
                first = (0, 2 * D, 3 * D)[a]
                if a == 0:
                    pe.wait_ge(qk_high, 2 * (8 * b + h + 1))
                    pe.wait_ge(qk_low, 8 * b + h + 1)
                aux_free(b, s)
                for nt in range(NT):
                    mm = pe.transpose(ps_aux16[:, nt * P:(nt + 1) * P],
                                      qk_pair[:, nt, h % 2, first:first + 2 * D], ident16[:, :])
                mm.then_inc(qk_turned, 1)

            def score(b, t):
                h, half, k = t // HEAD_SLOTS, t // UNIT_SLOTS % 2, t % UNIT_SLOTS
                if t % HEAD_SLOTS == 0:
                    pe.wait_ge(qkT_copied, 3 * (8 * b + h + 1))
                after(pe, exp_done, SLOTS * b + t - 1)
                q = qkT[:, h % 2, 0, half * NH:(half + 1) * NH]
                for jj in range(2):
                    keys = slice((2 * k + jj) * P, (2 * k + jj + 1) * P)
                    pe.matmul(ps_score[:, t % 2, jj, :], qkT[:, h % 2, 1, keys], q, start=True, stop=False)
                    mm = pe.matmul(ps_score[:, t % 2, jj, :], qkT[:, h % 2, 2, keys], q,
                                   start=False, stop=True)
                mm.then_inc(scores_done, 1)

            def attend(b, t):
                u, it = t // 4, t % 4
                h = u // 2
                if it == 0:
                    pe.wait_ge(probs_low, 4 * (16 * b + u + 1))
                    pe.wait_ge(v_high, 8 * b + h + 1)
                    pe.wait_ge(v_low, 8 * b + h + 1)
                after(pe, pv_added, SLOTS * b + t - 1)
                queries = slice(it * P, (it + 1) * P)
                for jt in range(NT):
                    parts = [(0, VCOLS), (1, D + 1)]
                    if jt == NT - 1:
                        parts.reverse()
                    for part, cols in parts:
                        mm = pe.matmul(ps_pv[:, t % 2, 0:cols], probs[:, u % 2, part, jt, queries],
                                       v_pair[:, h % 4, jt, 0:cols], start=(jt == 0 and part == 0),
                                       stop=(jt == NT - 1 and part == 0))
                mm.then_inc(pv_done, 1)

            def turn_res(b, m, s):
                p, part = m // 2, m % 2
                pe.wait_ge(res_low, 16 * b + 4 * (p + 1))
                aux_free(b, s)
                for it in range(NT):
                    mm = pe.transpose(ps_aux16[:, it * P:(it + 1) * P], res_pair[:, part, it, :],
                                      ident16[:, :])
                mm.then_inc(res_turned, 1)

            def project_out(b, k, s):
                if k == 0:
                    pe.wait_ge(resT_copied, 8 * (b + 1))
                aux_free(b, s)
                rows, pix = slice((k // 2) * P, (k // 2 + 1) * P), slice((k % 2) * NH, (k % 2 + 1) * NH)
                for ct in range(CT):
                    pe.matmul(ps_aux[:, :], woT_hi[:, ct, rows], resT[:, 0, ct, pix],
                              start=(ct == 0), stop=False)
                    pe.matmul(ps_aux[:, :], woT_hi[:, ct, rows], resT[:, 1, ct, pix],
                              start=False, stop=False)
                    mm = pe.matmul(ps_aux[:, :], woT_lo[:, ct, rows], resT[:, 0, ct, pix],
                                   start=False, stop=(ct == CT - 1))
                mm.then_inc(out_done, 1)

            def task(b, s):
                if 0 <= s - PV_LAG < SLOTS:
                    attend(b, s - PV_LAG)
                if 0 <= s < SLOTS:
                    score(b, s)
                for n, at in enumerate(PROJ_AT):
                    if at == s:
                        project(b, n)
                for m, at in enumerate(TURN_QK_AT):
                    if at == s:
                        turn_qk(b, m, s)
                for m, at in enumerate(TURN_RES_AT):
                    if at == s:
                        turn_res(b, m, s)
                for k, at in enumerate(OUT_AT):
                    if at == s:
                        project_out(b, k, s)

            pe.wait_ge(ident_made, 4)
            for m in range(W_TILES):
                pe.wait_ge(w_scaled, m + 1)
                after(pe, w_low, m - 1)
                for ct in range(CT):
                    mm = pe.transpose(ps_score[:, m % 2, 0, ct * P:(ct + 1) * P],
                                      w_raw[:, m, ct * P:(ct + 1) * P], ident32[:, :])
                mm.then_inc(w_turned, 1)
            pe.wait_ge(w_high, W_TILES)
            pe.wait_ge(w_low, W_TILES)
            pe.wait_ge(consts_set, 4)
            timeline(pe, task)


_INS = {"x": "x", "L0_conv_w_proj": "w_proj", "L0_conv_w_out": "w_out"}


def kernel(**inputs):
    import concourse.bacc as _bacc
    from concourse.bass_utils import run_bass_kernel_spmd as _run

    nc = _bacc.Bacc("TRN2", target_bir_lowering=False, num_devices=1)
    arrays, args = {}, []
    for name, short in _INS.items():
        a = np.ascontiguousarray(inputs[name])
        arrays[f"in_{short}"] = a
        args.append(nc.dram_tensor(f"in_{short}", a.shape, mybir.dt.from_np(a.dtype),
                                   kind="ExternalInput").ap())
    args.append(nc.dram_tensor("out_0", (B, C, H, W), F32, kind="ExternalOutput").ap())
    prepare_and_attend(nc, *args)
    r = _run(nc, [arrays], core_ids=[0])
    return r.results[0]["out_0"]
```

```python
from contextlib import ExitStack
from math import sqrt

import numpy as np

import concourse.bass as bass
from concourse import mybir

F32 = mybir.dt.float32
F32R = mybir.dt.float32r
F16 = mybir.dt.float16
I32 = mybir.dt.int32
ACT = mybir.ActivationFunctionType
ALU = mybir.AluOpType
AX = mybir.AxisListType

P = 128
B, C, H, W = 16, 512, 32, 32
N = H * W
D = 64
HEADS = C // D
PAIRS = HEADS // 2
O3 = 3 * C
CT = C // P
NT = N // P
NH = 512
PAIR_O = 6 * D

EPS_W = 1e-4
EPS_PIX = 1e-8
B_CONTRIB = 0.3
A_C, B_C = np.float32(1.0 - B_CONTRIB), np.float32(B_CONTRIB)
DIV = float(np.sqrt(A_C * A_C + B_C * B_C, dtype=np.float32))
FAN_IN = float(np.sqrt(C, dtype=np.float32))
ALPHA = float(np.sqrt(1.0 / C, dtype=np.float32))
QK_SCALE = 1.0 / sqrt(sqrt(D))

QK_UP = 2.0 ** 10
V_UP = 2.0 ** 12
WO_UP = 2.0 ** 14
PROB_SHIFT = 3.0
RSQRT_SEED = 1597463007.0

SLOTS = 64
TICKS = 4
UNIT_SLOTS = 4
HEAD_SLOTS = 8
PAIR_SLOTS = 16


def ticks(*offsets):
    return [round(TICKS * (PAIR_SLOTS * p + o)) for p in range(PAIRS) for o in offsets]


SCORE, EXP, HIGH_P, LOW_P = 1, 2, 3, 3
PV_LAG = 5
ATTEND, COPY_LOW, ADD_LOW = 0, 1, 1
ACT_HIGH = (3,)
PROJ_STEP = 0.75
PROJ_AT = ticks(*[-24 + 0.5 + PROJ_STEP * i for i in range(2 * NT)])
PROJ_COPY_AT = [at + 1 for at in PROJ_AT[1::2]]
REDUCE_AT = [at + 3 for at in PROJ_AT[1::2]]
NORM_AT = ticks(-11.25)
NORM_STEPS = 16
SCALE_AT = ticks(-10, -9.5, -7.5, -6.75)
HIGH_AT = ticks(-9.25, -9, -6.25, -5.75)
LOW_AT = ticks(-8.75, -8.25, -7.75, -5.5, -5, -4.5)
TURN_QK_AT = ticks(-4, -3, -2, 0.5, 2, 3.5)
COPY_QKT_AT = [at + 1 for at in TURN_QK_AT]
SPLIT_RES_AT = [TICKS * (UNIT_SLOTS * u + PV_LAG + 3) + 3 for u in range(2 * HEADS)]
TURN_RES_AT = [round(TICKS * o) for o in (26.75, 27.25, 40.5, 41.25, 56.5, 57.25, 71.25, 72)]
COPY_RES_AT = [at + 1 for at in TURN_RES_AT]
OUT_AT = [round(TICKS * (SLOTS + o)) for k in (9.25, 10.75, 15, 20, 21.25, 22.5, 23.75, 25.25) for o in (k, k + 0.5)]
ADD_OUT_AT = [at + 3 for at in OUT_AT[1::2]]
FINISH_AT = [at + 4 for at in ADD_OUT_AT]
SPLIT_AT = [round(TICKS * o) for o in (-27, -26.5, -26, -25.5, -25, -24.75, -24.5, -24)]
X_HIGH_AT = [at - 2 for at in SPLIT_AT]
FIRST_TICK = -33 * TICKS
LAST_TICK = (SLOTS + 30) * TICKS


def prepare_and_attend(nc, x, w_proj, w_out, out):
    x_in = x.rearrange("b (t p) h w -> b t p (h w)", p=P)
    out_v = out.rearrange("b (t p) h w -> b t p (h w)", p=P)
    wp_in = w_proj.rearrange("(m p) c a b -> p m (c a b)", p=P)
    wo_in = w_out.rearrange("(m p) c a b -> p m (c a b)", p=P)
    WP_TILES, WO_TILES = O3 // P, C // P
    W_TILES = WP_TILES + WO_TILES
    W_GROUPS = W_TILES // 4

    with ExitStack() as ctx:
        def sb(name, shape, dt):
            return ctx.enter_context(nc.sbuf_tensor(name, shape, dt))

        def pb(name, shape, dt):
            return ctx.enter_context(nc.psum_tensor(name, shape, dt))

        def sem(name):
            return ctx.enter_context(nc.semaphore(name))

        wpT_hi = sb("wpT_hi", [P, CT, O3], F32R)
        wpT_lo = sb("wpT_lo", [P, CT, O3], F32R)
        woT_hi = sb("woT_hi", [P, CT, C], F16)
        woT_lo = sb("woT_lo", [P, CT, C], F16)
        ident16 = sb("ident16", [P, P], F16)
        x_raw = sb("x_raw", [P, 2, NH], F32)
        x_hi = sb("x_hi", [P, CT, N], F32R)
        x_lo = sb("x_lo", [P, CT, N], F32R)
        proj = sb("proj", [P, NT, PAIR_O], F32)
        squares = sb("squares", [P, 2, PAIR_O], F32)
        ident32 = squares[:, 0, 0:P]
        sumsq = sb("sumsq", [P, NT, 6], F32)
        rs = sb("rs", [P, NT, 6], F32)
        rs_t = sb("rs_t", [P, NT, 6], F32)
        rs_unit = sb("rs_unit", [P, NT, 6], F32)
        qk_pair = sb("qk_pair", [P, NT, 2, 5 * D], F16)
        qkT = sb("qkT", [P, 2, 3, N], F16)
        VCOLS = 2 * D + 1
        v_pair = sb("v_pair", [P, 4, NT, VCOLS + 1], F16)
        e_tile = sb("e_tile", [P, 2, 2, NH], F32)
        probs = sb("probs", [P, 2, 2, NT, NH], F16)
        pv_low = sb("pv_low", [P, 2, D], F32)
        pv_sum = sb("pv_sum", [P, 4, D], F32)
        inv_sum = sb("inv_sum", [P, 4], F32)
        res_pair = sb("res_pair", [P, 2, 2, NT, 2 * D], F16)
        resT = sb("resT", [P, 2, CT, N], F16)
        x_res = sb("x_res", [P, 2, NH], F32)
        shift = sb("shift", [P, 3], F32)
        w_sumsq = sb("w_sumsq", [P, W_TILES], F32)
        w_rs = sb("w_rs", [P, W_TILES], F32)
        w_rs_t = e_tile[:, 1, 0, 0:W_TILES]
        w_raw = probs[:, :, :, :, :].rearrange("p a b j n -> p (a b j n)").bitcast(F32) \
            .rearrange("p (m c) -> p m c", c=C)
        w_scratch = e_tile[:, 0, 0, :]

        ps_score = pb("ps_score", [P, 2, 2, NH], F32)
        ps_pv = pb("ps_pv", [P, 2, NH], F32)
        ps_proj = pb("ps_proj", [P, NH], F32)
        ps_aux = pb("ps_aux", [P, NH], F32)
        ps_aux16 = ps_aux[:, :].bitcast(F16)

        w_loaded = [sem(f"w_loaded{g}") for g in range(W_GROUPS)]
        ident_made = sem("ident_made")
        consts_set = sem("consts_set")
        w_squared = sem("w_squared")
        w_step = sem("w_step")
        w_scaled = sem("w_scaled")
        w_turned = sem("w_turned")
        w_high = sem("w_high")
        w_low = sem("w_low")
        x_loaded = [sem(f"x_loaded{i}") for i in range(2)]
        x_high = sem("x_high")
        x_split = sem("x_split")
        proj_done = sem("proj_done")
        squared = sem("squared")
        proj_copied = sem("proj_copied")
        reduced = sem("reduced")
        norm_step = sem("norm_step")
        scaled = sem("scaled")
        qk_high = sem("qk_high")
        v_high = sem("v_high")
        qk_low = sem("qk_low")
        v_low = sem("v_low")
        qk_turned = sem("qk_turned")
        qkT_copied = sem("qkT_copied")
        scores_done = sem("scores_done")
        exp_done = sem("exp_done")
        probs_high = sem("probs_high")
        probs_high_act = sem("probs_high_act")
        probs_low = sem("probs_low")
        pv_done = sem("pv_done")
        pv_low_copied = sem("pv_low_copied")
        pv_inverted = sem("pv_inverted")
        pv_added = sem("pv_added")
        res_scaled = sem("res_scaled")
        res_high = sem("res_high")
        res_low = sem("res_low")
        res_turned = sem("res_turned")
        resT_copied = sem("resT_copied")
        out_done = sem("out_done")
        x_res_loaded = [sem(f"x_res_loaded{i}") for i in range(2)]
        out_added = sem("out_added")
        out_scaled = sem("out_scaled")
        out_stored = [sem(f"out_stored{i}") for i in range(2)]

        def after(eng, semaphore, count):
            if isinstance(count, int) and count <= 0:
                return
            eng.wait_ge(semaphore, count)

        def timeline(eng, task):
            span = SLOTS * TICKS

            def body(b, prev=True, cur=True, nxt=True):
                for s in range(span):
                    if prev and s + span <= LAST_TICK:
                        task(b - 1, s + span)
                    if cur:
                        task(b, s)
                    if nxt and s - span >= FIRST_TICK:
                        task(b + 1, s - span)

            body(-1, prev=False, cur=False)
            body(0, prev=False)
            with eng.Fori(1, B - 1) as b:
                body(b)
            body(B - 1, nxt=False)
            body(B, cur=False, nxt=False)

        block = ctx.enter_context(nc.Block())

        @block.gpsimd
        def _(pool):
            pool.memset(ident32, 0.0).then_inc(ident_made, 1)
            pool.memset(ident16[:, :], 0.0).then_inc(ident_made, 1)
            pool.wait_ge(ident_made, 2)
            for t in (ident32, ident16[:, :]):
                pool.affine_select(out=t, in_=t, compare_op=ALU.not_equal, fill=1.0, base=0,
                                   pattern=[[-1, P]], channel_multiplier=1).then_inc(ident_made, 1)

            def norms(b, p):
                done = NORM_STEPS * (4 * b + p)
                y, a, t = rs[:, :, :], sumsq[:, :, :], rs_t[:, :, :]
                half, three_halves = (shift[:, c:c + 1].unsqueeze(2).broadcast_to([P, NT, 6]) for c in (1, 2))
                pool.wait_ge(norm_step, done + 2)
                pool.tensor_tensor(a, a, half, ALU.mult).then_inc(norm_step, 1)
                for i in range(3):
                    pool.wait_ge(norm_step, done + 4 * i + 3)
                    pool.tensor_tensor(t, y, y, ALU.mult).then_inc(norm_step, 1)
                    pool.wait_ge(norm_step, done + 4 * i + 4)
                    pool.tensor_tensor(t, t, a, ALU.mult).then_inc(norm_step, 1)
                    pool.wait_ge(norm_step, done + 4 * i + 5)
                    pool.tensor_tensor(t, t, three_halves, ALU.add).then_inc(norm_step, 1)
                    pool.wait_ge(norm_step, done + 4 * i + 6)
                    pool.tensor_tensor(y, t, y, ALU.mult).then_inc(norm_step, 1)
                pool.wait_ge(norm_step, done + 15)
                pool.tensor_tensor(y, y, rs_unit[:, :, :], ALU.mult).then_inc(norm_step, 1)

            def task(b, s):
                for p, at in enumerate(NORM_AT):
                    if at == s:
                        norms(b, p)

            pool.wait_ge(consts_set, 6)
            timeline(pool, task)

        @block.sync
        def _(sp):
            def load_x(b, piece):
                n = 8 * b + piece
                after(sp, x_split, n - 1)
                sp.dma_start(x_raw[:, piece % 2, :],
                             x_in[bass.ds(b, 1), piece // 2, :, (piece % 2) * NH:(piece % 2 + 1) * NH]
                             .rearrange("a p n -> p (a n)")).then_inc(x_loaded[piece % 2], 16)

            def load_residual(b, k):
                after(sp, out_stored[k % 2], 16 * (4 * b + k // 2))
                sp.dma_start(x_res[:, k % 2, :],
                             x_in[bass.ds(b, 1), k // 2, :, (k % 2) * NH:(k % 2 + 1) * NH]
                             .rearrange("a p n -> p (a n)")).then_inc(x_res_loaded[k % 2], 16)

            def store(b, k):
                sp.wait_ge(out_scaled, 8 * b + k + 1)
                sp.dma_start(out_v[bass.ds(b, 1), k // 2, :, (k % 2) * NH:(k % 2 + 1) * NH]
                             .rearrange("a p n -> p (a n)"),
                             x_res[:, k % 2, :]).then_inc(out_stored[k % 2], 16)

            def task(b, s):
                for piece, at in enumerate(SPLIT_AT):
                    if at - 2 * TICKS == s:
                        load_x(b, piece)
                if s == OUT_AT[0] - 4 * TICKS:
                    load_residual(b, 0)
                    load_residual(b, 1)
                for k, at in enumerate(FINISH_AT):
                    if at + 1 == s:
                        store(b, k)
                        if k + 2 < len(FINISH_AT):
                            load_residual(b, k + 2)

            for g in range(W_GROUPS):
                src = wp_in[:, 4 * g:4 * g + 4, :] if 4 * g < WP_TILES else wo_in
                sp.dma_start(w_raw[:, 4 * g:4 * g + 4, :], src).then_inc(w_loaded[g], 16)
            timeline(sp, task)
            for i in range(2):
                sp.wait_ge(out_stored[i], 16 * 4 * B)

        @block.scalar
        def _(act):
            def square(b, n):
                act.wait_ge(proj_done, 32 * b + n + 1)
                after(act, reduced, 32 * b + n - 1)
                act.activation(squares[:, n % 2, :], ps_proj[:, 0:PAIR_O], ACT.Square).then_inc(squared, 1)

            def copy_proj(b, n):
                if n % (NT // 2) == 0:
                    done = 8 * b + n // (NT // 2) - 1
                    after(act, qk_low, 2 * done)
                    after(act, v_low, done)
                act.activation(proj[:, n % NT, :], ps_proj[:, 0:PAIR_O], ACT.Copy).then_inc(proj_copied, 1)

            def high(b, j, part):
                p, tiles = j // 2, slice((j % 2) * NT // 2, (j % 2 + 1) * NT // 2)
                src = proj[:, tiles, :].rearrange("p n (h g d) -> p n h g d", g=3, d=D)
                dst = qk_pair[:, tiles, :, :]
                if part == 0:
                    act.wait_ge(scaled, 2 * (8 * b + j + 1))
                    after(act, qk_turned, 6 * (4 * b + p))
                    act.activation(dst[:, :, :, 0:D], src[:, :, :, 0, :], ACT.Copy).then_inc(qk_high, 1)
                    after(act, pv_done, PAIR_SLOTS * (4 * b + p - 1))
                    heads = slice(2 * (p % 2), 2 * (p % 2) + 2)
                    act.activation(v_pair[:, heads, tiles, 0:D].rearrange("p h n d -> p n h d"),
                                   src[:, :, :, 2, :], ACT.Copy).then_inc(v_high, 1)
                else:
                    for hh in range(2):
                        twice = dst[:, :, hh, D:5 * D].rearrange("p n (e g d) -> p n e g d", g=2, d=D)
                        act.activation(twice[:, :, :, 1, :],
                                       src[:, :, hh, 1:2, :].broadcast_to([P, NT // 2, 2, D]),
                                       ACT.Copy).then_inc(qk_high, 1)

            def copy_qkT(b, m):
                h, a = m // 3, m % 3
                act.wait_ge(qk_turned, 24 * b + m + 1)
                after(act, scores_done, 8 * (8 * b + h - 1))
                act.activation(qkT[:, h % 2, a, :], ps_aux16, ACT.Copy).then_inc(qkT_copied, 1)

            def exp(b, t):
                act.wait_ge(scores_done, SLOTS * b + t + 1)
                after(act, probs_low, SLOTS * b + t - 1)
                act.activation(e_tile[:, t % 2, :, :], ps_score[:, t % 2, :, :], ACT.Exp,
                               bias=shift[:, 0:1], scale=1.0 / (QK_UP * QK_UP)).then_inc(exp_done, 1)

            def high_probs(b, t):
                u, k = t // UNIT_SLOTS, t % UNIT_SLOTS
                after(act, pv_done, UNIT_SLOTS * (16 * b + u - 1))
                act.wait_ge(exp_done, SLOTS * b + t + 1)
                act.activation(probs[:, u % 2, 0, 2 * k:2 * k + 2, :], e_tile[:, t % 2, :, :],
                               ACT.Copy).then_inc(probs_high_act, 1)

            def high_x(b, piece):
                ct, half = piece // 2, slice((piece % 2) * NH, (piece % 2 + 1) * NH)
                act.wait_ge(x_loaded[piece % 2], 16 * (4 * b + piece // 2 + 1))
                after(act, proj_done, 32 * b)
                act.activation(x_hi[:, ct, half], x_raw[:, piece % 2, :], ACT.Copy).then_inc(x_high, 1)

            def copy_resT(b, m):
                act.wait_ge(res_turned, 8 * b + m + 1)
                after(act, out_done, 8 * b)
                act.activation(resT[:, m % 2, m // 2, :], ps_aux16, ACT.Copy).then_inc(resT_copied, 1)

            def copy_low(b, t):
                act.wait_ge(pv_done, SLOTS * b + t + 1)
                after(act, pv_added, SLOTS * b + t - 1)
                act.activation(pv_low[:, t % 2, :], ps_pv[:, t % 2, D + 1:VCOLS], ACT.Copy) \
                    .then_inc(pv_low_copied, 1)

            def finish(b, k):
                act.wait_ge(out_added, 8 * b + k + 1)
                act.activation(x_res[:, k % 2, :], x_res[:, k % 2, :], ACT.Copy,
                               scale=float(A_C) / DIV).then_inc(out_scaled, 1)

            def task(b, s):
                slot, tick = divmod(s, TICKS)
                if 0 <= slot - PV_LAG < SLOTS and tick == COPY_LOW:
                    copy_low(b, slot - PV_LAG)
                if 0 <= slot < SLOTS and tick == EXP:
                    exp(b, slot)
                if 0 <= slot < SLOTS and tick == HIGH_P and slot % UNIT_SLOTS in ACT_HIGH:
                    high_probs(b, slot)
                for n, at in enumerate(PROJ_COPY_AT):
                    if at == s:
                        square(b, n)
                        copy_proj(b, n)
                for j, at in enumerate(HIGH_AT):
                    if at == s:
                        high(b, j // 2, j % 2)
                for m, at in enumerate(COPY_QKT_AT):
                    if at == s:
                        copy_qkT(b, m)
                for m, at in enumerate(COPY_RES_AT):
                    if at == s:
                        copy_resT(b, m)
                for k, at in enumerate(FINISH_AT):
                    if at == s:
                        finish(b, k)
                for piece, at in enumerate(X_HIGH_AT):
                    if at == s:
                        high_x(b, piece)

            for m in range(W_TILES):
                act.wait_ge(w_loaded[m // 4], 16)
                if m:
                    act.wait_ge(w_squared, m)
                act.activation(w_scratch, w_raw[:, m, :], ACT.Square,
                               accum_out=w_sumsq[:, m:m + 1]).then_inc(w_squared, 1)
            for m in range(W_TILES):
                act.wait_ge(w_turned, m + 1)
                turned = ps_score[:, m % 2, 0, :].rearrange("p (t o) -> p t o", o=P)
                if m < WP_TILES:
                    act.activation(wpT_hi[:, :, m * P:(m + 1) * P], turned, ACT.Copy).then_inc(w_high, 1)
                else:
                    o = (m - WP_TILES) * P
                    act.activation(woT_hi[:, :, o:o + P], turned, ACT.Copy, scale=WO_UP).then_inc(w_high, 1)
            act.wait_ge(consts_set, 6)
            timeline(act, task)

        @block.vector
        def _(dve):
            def rsqrt_seed(y, a, step):
                dve.tensor_scalar(y.bitcast(I32), a.bitcast(I32), -0.5, RSQRT_SEED, ALU.mult, ALU.add) \
                   .then_inc(step, 1)

            def rsqrt_newton(y, a, t, step, done, first, end):
                for i in range(first, end):
                    dve.wait_ge(step, done + 3 * i)
                    dve.tensor_tensor(t, y, y, ALU.mult).then_inc(step, 1)
                    dve.wait_ge(step, done + 3 * i + 1)
                    dve.scalar_tensor_tensor(out=t, in0=t, scalar=-0.5, in1=a, op0=ALU.mult,
                                             op1=ALU.mult).then_inc(step, 1)
                    dve.wait_ge(step, done + 3 * i + 2)
                    dve.scalar_tensor_tensor(out=y, in0=t, scalar=1.5, in1=y, op0=ALU.add,
                                             op1=ALU.mult).then_inc(step, 1)
            RSQRT_STEPS = 10

            def split_x(b, piece):
                n = 8 * b + piece
                ct, half = piece // 2, slice((piece % 2) * NH, (piece % 2 + 1) * NH)
                dve.wait_ge(x_high, n + 1)
                dve.tensor_tensor(x_lo[:, ct, half], x_raw[:, piece % 2, :],
                                  x_hi[:, ct, half].bitcast(F32), ALU.subtract).then_inc(x_split, 1)

            def reduce(b, n):
                dve.wait_ge(squared, 32 * b + n + 1)
                if n % NT == 0:
                    after(dve, norm_step, NORM_STEPS * (4 * b + n // NT))
                dve.tensor_reduce(sumsq[:, n % NT, :],
                                  squares[:, n % 2, :].rearrange("p (g d) -> p g d", d=D), AX.X,
                                  ALU.add).then_inc(reduced, 1)

            def seed_norms(b, p):
                dve.wait_ge(reduced, 32 * b + NT * (p + 1))
                after(dve, scaled, 4 * (4 * b + p))
                dve.tensor_scalar(sumsq[:, :, :], sumsq[:, :, :], D * EPS_PIX, None, ALU.add) \
                   .then_inc(norm_step, 1)
                dve.wait_ge(norm_step, NORM_STEPS * (4 * b + p) + 1)
                rsqrt_seed(rs[:, :, :], sumsq[:, :, :], norm_step)

            def scale(b, j):
                p, tiles = j // 4, slice(2 * (j % 4), 2 * (j % 4) + 2)
                dve.wait_ge(proj_copied, 32 * b + NT * (p + 1))
                dve.wait_ge(norm_step, NORM_STEPS * (4 * b + p + 1))
                v = proj[:, tiles, :].rearrange("p n (g d) -> p n g d", d=D)
                r = rs[:, tiles, :].unsqueeze(3).broadcast_to([P, 2, 6, D])
                dve.tensor_tensor(v, v, r, ALU.mult).then_inc(scaled, 1)

            def low(b, j, part):
                p, tiles = j // 2, slice((j % 2) * NT // 2, (j % 2 + 1) * NT // 2)
                src = proj[:, tiles, :].rearrange("p n (h g d) -> p n h g d", g=3, d=D)
                if part < 2:
                    dst = qk_pair[:, tiles, part, 0:4 * D].rearrange("p n (g e d) -> p n g e d", e=2, d=D)
                    dve.wait_ge(qk_high, 3 * (8 * b + j + 1))
                    dve.tensor_tensor(dst[:, :, :, 1, :], src[:, :, part, 0:2, :], dst[:, :, :, 0, :],
                                      ALU.subtract).then_inc(qk_low, 1)
                else:
                    heads = slice(2 * (p % 2), 2 * (p % 2) + 2)
                    dve.wait_ge(v_high, 8 * b + j + 1)
                    v = v_pair[:, heads, tiles, :].rearrange("p h n d -> p n h d")
                    dve.tensor_tensor(v[:, :, :, D + 1:VCOLS], src[:, :, :, 2, :], v[:, :, :, 0:D],
                                      ALU.subtract).then_inc(v_low, 1)

            dve_high = [k for k in range(UNIT_SLOTS) if k not in ACT_HIGH]

            def split_probs_high(b, t):
                u, k = t // UNIT_SLOTS, t % UNIT_SLOTS
                dve.wait_ge(exp_done, SLOTS * b + t + 1)
                after(dve, pv_done, UNIT_SLOTS * (16 * b + u - 1))
                dve.tensor_copy(probs[:, u % 2, 0, 2 * k:2 * k + 2, :], e_tile[:, t % 2, :, :]) \
                   .then_inc(probs_high, 1)

            def split_probs_low(b, t):
                u, k = t // UNIT_SLOTS, t % UNIT_SLOTS
                if k in ACT_HIGH:
                    dve.wait_ge(probs_high_act, len(ACT_HIGH) * (16 * b + u) + ACT_HIGH.index(k) + 1)
                else:
                    dve.wait_ge(probs_high, len(dve_high) * (16 * b + u) + dve_high.index(k) + 1)
                dve.tensor_tensor(probs[:, u % 2, 1, 2 * k:2 * k + 2, :], e_tile[:, t % 2, :, :],
                                  probs[:, u % 2, 0, 2 * k:2 * k + 2, :], ALU.subtract) \
                   .then_inc(probs_low, 1)

            def add_low(b, t):
                it = t % 4
                if it == 0:
                    after(dve, res_low, 16 * b + t // 4)
                dve.wait_ge(pv_low_copied, SLOTS * b + t + 1)
                dve.reciprocal(inv_sum[:, it:it + 1], ps_pv[:, t % 2, D:D + 1]).then_inc(pv_inverted, 1)
                dve.tensor_tensor(pv_sum[:, it, :], ps_pv[:, t % 2, 0:D], pv_low[:, t % 2, :],
                                  ALU.add).then_inc(pv_added, 1)

            def split_res(b, u):
                h, half = u // 2, u % 2
                cols = slice((h % 2) * D, (h % 2 + 1) * D)
                dve.wait_ge(pv_added, 4 * (16 * b + u + 1))
                dve.wait_ge(pv_inverted, 4 * (16 * b + u + 1))
                if u % 4 == 0:
                    after(dve, res_turned, 2 * (4 * b + u // 4 - 1))
                dve.tensor_tensor(pv_sum[:, :, :], pv_sum[:, :, :],
                                  inv_sum[:, :].unsqueeze(2).broadcast_to([P, 4, D]),
                                  ALU.mult).then_inc(res_scaled, 1)
                dve.wait_ge(res_scaled, 16 * b + u + 1)
                dve.tensor_copy(res_pair[:, u // 4 % 2, 0, 4 * half:4 * half + 4, cols], pv_sum[:, :, :]) \
                   .then_inc(res_high, 1)
                dve.wait_ge(res_high, 16 * b + u + 1)
                dve.tensor_tensor(res_pair[:, u // 4 % 2, 1, 4 * half:4 * half + 4, cols], pv_sum[:, :, :],
                                  res_pair[:, u // 4 % 2, 0, 4 * half:4 * half + 4, cols],
                                  ALU.subtract).then_inc(res_low, 1)

            def add_out(b, k):
                dve.wait_ge(out_done, 8 * b + k + 1)
                dve.wait_ge(x_res_loaded[k % 2], 16 * (4 * b + k // 2 + 1))
                dve.scalar_tensor_tensor(out=x_res[:, k % 2, :], in0=ps_aux[:, :],
                                         scalar=float(B_C) / float(A_C) / (V_UP * WO_UP),
                                         in1=x_res[:, k % 2, :], op0=ALU.mult,
                                         op1=ALU.add).then_inc(out_added, 1)

            def task(b, s):
                slot, tick = divmod(s, TICKS)
                if 0 <= slot - PV_LAG < SLOTS and tick == ADD_LOW:
                    add_low(b, slot - PV_LAG)
                for n, at in enumerate(REDUCE_AT):
                    if at == s:
                        reduce(b, n)
                for p, at in enumerate(NORM_AT):
                    if at == s:
                        seed_norms(b, p)
                for j, at in enumerate(SCALE_AT):
                    if at == s:
                        scale(b, j)
                for j, at in enumerate(LOW_AT):
                    if at == s:
                        low(b, j // 3, j % 3)
                for k, at in enumerate(ADD_OUT_AT):
                    if at == s:
                        add_out(b, k)
                for piece, at in enumerate(SPLIT_AT):
                    if at == s:
                        split_x(b, piece)
                for u, at in enumerate(SPLIT_RES_AT):
                    if at == s:
                        split_res(b, u)
                if 0 <= slot < SLOTS and tick == HIGH_P and slot % UNIT_SLOTS not in ACT_HIGH:
                    split_probs_high(b, slot)
                if 0 <= slot < SLOTS and tick == LOW_P:
                    split_probs_low(b, slot)

            dve.memset(v_pair[:, :, :, D:D + 1], 1.0).then_inc(consts_set, 1)
            for c, value in enumerate((PROB_SHIFT, -0.5, 1.5)):
                dve.memset(shift[:, c:c + 1], value).then_inc(consts_set, 1)
            unit = rs_unit[:, :, :].rearrange("p n (h g) -> p (n h) g", g=3)
            dve.memset(unit[:, :, 0:2], sqrt(D) * QK_SCALE * QK_UP).then_inc(consts_set, 1)
            dve.memset(unit[:, :, 2:3], sqrt(D) * V_UP).then_inc(consts_set, 1)
            dve.wait_ge(consts_set, 6)
            dve.wait_ge(w_squared, W_TILES)
            dve.tensor_scalar(w_sumsq[:, :], w_sumsq[:, :], 1e-30, None, ALU.max).then_inc(w_step, 1)
            dve.wait_ge(w_step, 1)
            rsqrt_seed(w_rs[:, :], w_sumsq[:, :], w_step)
            rsqrt_newton(w_rs[:, :], w_sumsq[:, :], w_rs_t, w_step, 2, 0, 3)
            n = 1 + RSQRT_STEPS
            dve.wait_ge(w_step, n)
            dve.tensor_tensor(w_rs[:, :], w_rs[:, :], w_sumsq[:, :], ALU.mult).then_inc(w_step, 1)
            dve.wait_ge(w_step, n + 1)
            dve.tensor_scalar(w_rs[:, :], w_rs[:, :], ALPHA, EPS_W, ALU.mult, ALU.add).then_inc(w_step, 1)
            dve.wait_ge(w_step, n + 2)
            dve.tensor_scalar(w_rs[:, :], w_rs[:, :], FAN_IN, None, ALU.mult).then_inc(w_step, 1)
            dve.wait_ge(w_step, n + 3)
            dve.reciprocal(w_rs[:, :], w_rs[:, :]).then_inc(w_step, 1)
            dve.wait_ge(w_step, n + 4)
            for m in range(W_TILES):
                dve.tensor_scalar(w_raw[:, m, :], w_raw[:, m, :], w_rs[:, m:m + 1], None,
                                  ALU.mult).then_inc(w_scaled, 1)
            for m in range(W_TILES):
                dve.wait_ge(w_high, m + 1)
                turned = ps_score[:, m % 2, 0, :].rearrange("p (t o) -> p t o", o=P)
                if m < WP_TILES:
                    cols = slice(m * P, (m + 1) * P)
                    dve.tensor_tensor(wpT_lo[:, :, cols], turned, wpT_hi[:, :, cols].bitcast(F32),
                                      ALU.subtract).then_inc(w_low, 1)
                else:
                    cols = slice((m - WP_TILES) * P, (m - WP_TILES + 1) * P)
                    dve.scalar_tensor_tensor(out=woT_lo[:, :, cols], in0=turned, scalar=WO_UP,
                                             in1=woT_hi[:, :, cols], op0=ALU.mult,
                                             op1=ALU.subtract).then_inc(w_low, 1)
            dve.wait_ge(w_turned, W_TILES)
            timeline(dve, task)

        @block.tensor
        def _(pe):
            def project(b, n, part):
                p, nt = n // NT, n % NT
                if n == 0 and part == 0:
                    pe.wait_ge(x_split, 8 * (b + 1))
                if part == 0:
                    after(pe, proj_copied, 32 * b + n)
                pix, cols = slice(nt * P, (nt + 1) * P), slice(p * PAIR_O, (p + 1) * PAIR_O)
                for ct in range(part * CT // 2, (part + 1) * CT // 2):
                    pe.matmul(ps_proj[:, 0:PAIR_O], x_hi[:, ct, pix], wpT_hi[:, ct, cols],
                              start=(ct == 0), stop=False)
                    pe.matmul(ps_proj[:, 0:PAIR_O], x_hi[:, ct, pix], wpT_lo[:, ct, cols],
                              start=False, stop=False)
                    mm = pe.matmul(ps_proj[:, 0:PAIR_O], x_lo[:, ct, pix], wpT_hi[:, ct, cols],
                                   start=False, stop=(ct == CT - 1))
                if part == 1:
                    mm.then_inc(proj_done, 1)

            def aux_free(b, s):
                users = [(at, qkT_copied, 24, m + 1) for m, at in enumerate(TURN_QK_AT)]
                users += [(at, resT_copied, 8, m + 1) for m, at in enumerate(TURN_RES_AT)]
                users += [(at, out_added, 8, k + 1) for k, at in enumerate(OUT_AT[0::2])]
                past = [(at + SLOTS * TICKS * e, copied, per, count, e) for at, copied, per, count in users
                        for e in (-1, 0, 1) if at + SLOTS * TICKS * e < s
                        and not (isinstance(b, int) and not 0 <= b + e < B)]
                if past:
                    at, copied, per, count, e = max(past, key=lambda u: u[0])
                    pe.wait_ge(copied, per * (b + e) + count)

            def turn_qk(b, m, s):
                h, a = m // 3, m % 3
                first = (0, 2 * D, 3 * D)[a]
                if a == 0:
                    pe.wait_ge(qk_high, 6 * (4 * b + h // 2 + 1))
                    pe.wait_ge(qk_low, 4 * (4 * b + h // 2 + 1))
                aux_free(b, s)
                for nt in range(NT):
                    mm = pe.transpose(ps_aux16[:, nt * P:(nt + 1) * P],
                                      qk_pair[:, nt, h % 2, first:first + 2 * D], ident16[:, :])
                mm.then_inc(qk_turned, 1)

            def score(b, t):
                h, half, k = t // HEAD_SLOTS, t // UNIT_SLOTS % 2, t % UNIT_SLOTS
                if t % HEAD_SLOTS == 0:
                    pe.wait_ge(qkT_copied, 3 * (8 * b + h + 1))
                after(pe, exp_done, SLOTS * b + t - 1)
                q = qkT[:, h % 2, 0, half * NH:(half + 1) * NH]
                for jj in range(2):
                    keys = slice((2 * k + jj) * P, (2 * k + jj + 1) * P)
                    pe.matmul(ps_score[:, t % 2, jj, :], qkT[:, h % 2, 1, keys], q, start=True, stop=False)
                    mm = pe.matmul(ps_score[:, t % 2, jj, :], qkT[:, h % 2, 2, keys], q,
                                   start=False, stop=True)
                mm.then_inc(scores_done, 1)

            def attend(b, t):
                u, it = t // 4, t % 4
                h = u // 2
                if it == 0:
                    pe.wait_ge(probs_low, 4 * (16 * b + u + 1))
                    pe.wait_ge(v_high, 2 * (4 * b + h // 2 + 1))
                    pe.wait_ge(v_low, 2 * (4 * b + h // 2 + 1))
                after(pe, pv_added, SLOTS * b + t - 1)
                queries = slice(it * P, (it + 1) * P)
                for jt in range(NT):
                    parts = [(0, VCOLS), (1, D + 1)]
                    if jt == NT - 1:
                        parts.reverse()
                    for part, cols in parts:
                        mm = pe.matmul(ps_pv[:, t % 2, 0:cols], probs[:, u % 2, part, jt, queries],
                                       v_pair[:, h % 4, jt, 0:cols], start=(jt == 0 and part == 0),
                                       stop=(jt == NT - 1 and part == 0))
                mm.then_inc(pv_done, 1)

            def turn_res(b, m, s):
                p, part = m // 2, m % 2
                pe.wait_ge(res_low, 16 * b + 4 * (p + 1))
                aux_free(b, s)
                for it in range(NT):
                    mm = pe.transpose(ps_aux16[:, it * P:(it + 1) * P], res_pair[:, p % 2, part, it, :],
                                      ident16[:, :])
                mm.then_inc(res_turned, 1)

            def project_out(b, k, part, s):
                if k == 0 and part == 0:
                    pe.wait_ge(resT_copied, 8 * (b + 1))
                if part == 0:
                    aux_free(b, s)
                rows, pix = slice((k // 2) * P, (k // 2 + 1) * P), slice((k % 2) * NH, (k % 2 + 1) * NH)
                for ct in range(part * CT // 2, (part + 1) * CT // 2):
                    pe.matmul(ps_aux[:, :], woT_hi[:, ct, rows], resT[:, 0, ct, pix],
                              start=(ct == 0), stop=False)
                    pe.matmul(ps_aux[:, :], woT_hi[:, ct, rows], resT[:, 1, ct, pix],
                              start=False, stop=False)
                    mm = pe.matmul(ps_aux[:, :], woT_lo[:, ct, rows], resT[:, 0, ct, pix],
                                   start=False, stop=(ct == CT - 1))
                if part == 1:
                    mm.then_inc(out_done, 1)

            def task(b, s):
                slot, tick = divmod(s, TICKS)
                if 0 <= slot - PV_LAG < SLOTS and tick == ATTEND:
                    attend(b, slot - PV_LAG)
                if 0 <= slot < SLOTS and tick == SCORE:
                    score(b, slot)
                for j, at in enumerate(PROJ_AT):
                    if at == s:
                        project(b, j // 2, j % 2)
                for m, at in enumerate(TURN_QK_AT):
                    if at == s:
                        turn_qk(b, m, s)
                for m, at in enumerate(TURN_RES_AT):
                    if at == s:
                        turn_res(b, m, s)
                for j, at in enumerate(OUT_AT):
                    if at == s:
                        project_out(b, j // 2, j % 2, s)

            pe.wait_ge(ident_made, 4)
            for m in range(W_TILES):
                pe.wait_ge(w_scaled, m + 1)
                after(pe, w_low, m - 1)
                for ct in range(CT):
                    mm = pe.transpose(ps_score[:, m % 2, 0, ct * P:(ct + 1) * P],
                                      w_raw[:, m, ct * P:(ct + 1) * P], ident32)
                mm.then_inc(w_turned, 1)
            pe.wait_ge(w_high, W_TILES)
            pe.wait_ge(w_low, W_TILES)
            pe.wait_ge(consts_set, 6)
            timeline(pe, task)


_INS = {"x": "x", "L0_conv_w_proj": "w_proj", "L0_conv_w_out": "w_out"}


def kernel(**inputs):
    import concourse.bacc as _bacc
    from concourse.bass_utils import run_bass_kernel_spmd as _run

    nc = _bacc.Bacc("TRN2", target_bir_lowering=False, num_devices=1)
    arrays, args = {}, []
    for name, short in _INS.items():
        a = np.ascontiguousarray(inputs[name])
        arrays[f"in_{short}"] = a
        args.append(nc.dram_tensor(f"in_{short}", a.shape, mybir.dt.from_np(a.dtype),
                                   kind="ExternalInput").ap())
    args.append(nc.dram_tensor("out_0", (B, C, H, W), F32, kind="ExternalOutput").ap())
    prepare_and_attend(nc, *args)
    r = _run(nc, [arrays], core_ids=[0])
    return r.results[0]["out_0"]
```
